# Optimizing a Trainium2 kernel written in Bass

```python
import numpy as np
import jax
import jax.numpy as jnp

def _softmax(x, axis=-1):
    return jax.nn.softmax(x, axis=axis)

def _gelu(x):
    return jax.nn.gelu(x, approximate=True)

def _silu(x):
    return jax.nn.silu(x)

def _sigmoid(x):
    return jax.nn.sigmoid(x)

def _layernorm(x, axis=-1, eps=1e-05):
    m = jnp.mean(x, axis=axis, keepdims=True)
    v = jnp.var(x, axis=axis, keepdims=True)
    return (x - m) / jnp.sqrt(v + eps)

def _scatter_add(tgt, idx, src, axis=0):
    return tgt.at[idx].add(src)

def _segment_sum(src, seg, n):
    return jax.ops.segment_sum(src, seg, n)
kernel_name = 'mk_adj_resnorm_d1_adj_r2_8c7bab'

def setup_inputs(seed: int=0):
    np.random.seed(seed)
    _w = jnp.asarray

    def _rec_inputs():
        import jax
        import jax.numpy as jnp
        _gk = jax.random.key(seed)
        x = 7.22e-05 + 1 * jax.random.normal(jax.random.fold_in(_gk, 1), (4096, 512), jnp.float32)
        _a = jax.random.bernoulli(jax.random.fold_in(_gk, 2), 0.00195312, (4096, 4096))
        _a = jnp.logical_or(_a, jnp.swapaxes(_a, -1, -2))
        _a = jnp.logical_or(_a, jnp.eye(4096, dtype=bool))
        _af = _a.astype(jnp.float32)
        _af = _af * jax.random.uniform(jax.random.fold_in(_gk, 3), (4096, 4096), jnp.float32, 0.05, 1)
        adj = _af
        return (x, adj)
    x, adj = _rec_inputs()

    def _L0_gnn_setup():
        import jax, jax.numpy as jnp
        import numpy as np
        N = 4096
        IN_FEATURES = 512
        OUT_FEATURES = 512
        key = jax.random.key(seed)
        k_x, k_adj, k_w, k_b = jax.random.split(key, 4)
        x = jax.random.normal(k_x, (N, IN_FEATURES), dtype=jnp.float32)
        adj = jax.random.uniform(k_adj, (N, N), dtype=jnp.float32)
        stdv = 1.0 / np.sqrt(OUT_FEATURES)
        weight = jax.random.uniform(k_w, (IN_FEATURES, OUT_FEATURES), dtype=jnp.float32, minval=-stdv, maxval=stdv)
        bias = jax.random.uniform(k_b, (OUT_FEATURES,), dtype=jnp.float32, minval=-stdv, maxval=stdv)
        return {'x': x, 'adj': adj, 'weight': weight, 'bias': bias}
    _L0_gnn_all = _L0_gnn_setup()
    _L0_gnn_in = {k: v for k, v in _L0_gnn_all.items() if k in ('weight', 'bias')}
    del _L0_gnn_all
    return {'x': x, 'adj': adj, 'L0_gnn_weight': _L0_gnn_in['weight'], 'L0_gnn_bias': _L0_gnn_in['bias']}

def reference(x, adj, L0_gnn_weight, L0_gnn_bias):
    import jax
    import jax.numpy as jnp

    def _L0_gnn_ref(x, adj, weight, bias):
        import jax, jax.numpy as jnp
        import numpy as np
        N = 4096
        IN_FEATURES = 512
        OUT_FEATURES = 512
        support = jnp.matmul(x, weight)
        output = jnp.matmul(adj, support)
        return output + bias
    x = _layernorm(x + _L0_gnn_ref(x, adj, L0_gnn_weight, L0_gnn_bias), axis=-1)
    return x

_drawn_inputs = setup_inputs


def setup_inputs(seed=0):
    import zlib

    import numpy as np

    out = dict(_drawn_inputs(seed))
    spreads = {}
    factors = {'L0_gnn_bias': 3.97}
    for name, (base, spread) in spreads.items():
        noise = np.random.default_rng([zlib.crc32(name.encode()), seed]).standard_normal(out[name].shape)
        drawn = base * np.exp(spread * noise) if base else spread * noise
        out[name] = jnp.asarray(drawn.astype(out[name].dtype))
    for name, factor in factors.items():
        out[name] = (out[name] * factor).astype(out[name].dtype)
    return out
```

```python
import concourse.bass as bass
from concourse import mybir
from contextlib import ExitStack

P = 128


def gnn_residual_layernorm(nc: bass.Bass, x: bass.AP, xT: bass.AP, adjT: bass.AP, weight: bass.AP,
                           bias: bass.AP, out: bass.AP):
    fp32 = mybir.dt.float32
    fp32r = mybir.dt.float32r
    ALU = mybir.AluOpType
    ACT = mybir.ActivationFunctionType

    N, F = x.shape
    ROWS = adjT.shape[3]
    TILES = ROWS // P
    KB = adjT.shape[2]
    GROUPS = N // ROWS
    X_CHUNKS = F // P // KB
    A_CHUNKS = N // P // KB
    RAW = 4
    PARTS = 2
    XN = GROUPS * X_CHUNKS
    EPS = 1e-5
    DMA = 16
    assert X_CHUNKS == PARTS and A_CHUNKS % RAW == 0 and XN % RAW == 0 and F <= 512

    ctx = ExitStack()
    with ctx:
        def sb(name, shape, dt=fp32):
            return ctx.enter_context(nc.sbuf_tensor(name, shape, dt))

        def sem(name):
            return ctx.enter_context(nc.semaphore(name))

        raw = sb("raw", [P, RAW, KB, ROWS])
        hi = sb("hi", [P, PARTS, KB, ROWS], fp32r)
        lo = sb("lo", [P, PARTS, KB, ROWS], fp32r)
        w_hi = sb("w_hi", [P, F // P, F], fp32r)
        w_lo = sb("w_lo", [P, F // P, F], fp32r)
        s_hi = sb("s_hi", [P, N // P, F], fp32r)
        s_lo = sb("s_lo", [P, N // P, F], fp32r)
        bias_all = sb("bias_all", [P, F])
        rows = sb("rows", [P, 2, TILES, F])
        w_raw = rows[:, 0]
        stats = sb("stats", [P, TILES, 6])
        mean_var = sb("mean_var", [P, TILES, 2])
        std = sb("std", [P, TILES, 1])
        rstd = sb("rstd", [P, TILES, 1])
        eps = sb("eps", [P, 1])
        acc = ctx.enter_context(nc.psum_tensor("acc", [P, 2, TILES, F], fp32))

        w_landed = [sem(f"w_landed{c}") for c in range(X_CHUNKS)]
        raw_landed = [sem(f"raw_landed{r}") for r in range(RAW)]
        bias_landed = sem("bias_landed")
        x_landed = sem("x_landed")
        w_hi_ready = sem("w_hi_ready")
        w_lo_ready = sem("w_lo_ready")
        hi_ready = sem("hi_ready")
        lo_ready = sem("lo_ready")
        tiles_multiplied = sem("tiles_multiplied")
        s_hi_ready = sem("s_hi_ready")
        banks_drained = sem("banks_drained")
        residual_ready = sem("residual_ready")
        eps_ready = sem("eps_ready")
        var_ready = sem("var_ready")
        std_ready = sem("std_ready")
        rstd_ready = sem("rstd_ready")
        normalized = sem("normalized")
        stored = sem("stored")
        last_stored = sem("last_stored")

        x_rows = x.rearrange("(g p t) f -> g p t f", p=P, t=TILES)
        out_rows = out.rearrange("(g p t) f -> g p t f", p=P, t=TILES)
        w_rows = weight.rearrange("(b p) f -> p b f", p=P)

        def x_complete(g, t):
            return g * (X_CHUNKS * TILES) + ((X_CHUNKS - 1) * TILES + t + 1)

        def a_complete(g, t):
            return g * (A_CHUNKS * TILES) + ((XN + A_CHUNKS - 1) * TILES + t + 1)

        block = ctx.enter_context(nc.Block())

        @block.sync
        def _(sp):
            for c in range(X_CHUNKS):
                sp.dma_start(w_raw[:, c * KB:(c + 1) * KB], w_rows[:, c * KB:(c + 1) * KB]).then_inc(w_landed[c], DMA)
                sp.dma_start(raw[:, c], xT[c]).then_inc(raw_landed[c], DMA)
            for r in range(X_CHUNKS, RAW):
                sp.dma_start(raw[:, r], xT[r]).then_inc(raw_landed[r], DMA)
            with sp.Fori(1, XN // RAW) as q:
                for r in range(RAW):
                    sp.wait_ge(lo_ready, q * RAW + (r + 1 - RAW))
                    sp.dma_start(raw[:, r], xT[q * RAW + r]).then_inc(raw_landed[r], DMA)
            with sp.Fori(0, GROUPS * A_CHUNKS // RAW) as q:
                for r in range(RAW):
                    sp.wait_ge(lo_ready, q * RAW + (XN + r + 1 - RAW))
                    sp.dma_start(raw[:, r], adjT[q * RAW + r]).then_inc(raw_landed[r], DMA)
            g = GROUPS - 1
            for t in range(TILES):
                sp.wait_ge(normalized, g * TILES + t + 1)
                sp.dma_start(out_rows[g, :, t], rows[:, g % 2, t]).then_inc(last_stored, DMA)
            sp.wait_ge(last_stored, TILES * DMA)

        @block.gpsimd
        def _(pool):
            nc.gpsimd.memset(eps[:], EPS).then_inc(eps_ready, 1)
            pool.dma_start(bias_all[:], bias.unsqueeze(0).to_broadcast([P, F])).then_inc(bias_landed, DMA)
            pool.wait_ge(bias_landed, DMA)
            pool.wait_ge(w_lo_ready, X_CHUNKS)

            def prepare(g, slot):
                pool.dma_start(rows[:, slot], x_rows[g]).then_inc(x_landed, DMA)
                pool.wait_ge(x_landed, (g + 1) * DMA)
                for t in range(TILES):
                    last = nc.gpsimd.tensor_tensor(rows[:, slot, t], rows[:, slot, t], bias_all[:], ALU.add)
                last.then_inc(residual_ready, 1)

            def store(g, slot):
                pool.wait_ge(normalized, (g + 1) * TILES)
                pool.dma_start(out_rows[g], rows[:, slot]).then_inc(stored, DMA)
                pool.wait_ge(stored, (g + 1) * DMA)

            prepare(0, 0)
            prepare(1, 1)
            with pool.Fori(0, GROUPS // 2 - 1) as i:
                for h in range(2):
                    store(i * 2 + h, h)
                    prepare(i * 2 + (2 + h), h)
            store(GROUPS - 2, 0)

        @block.scalar
        def _(act):
            def split(base, slot, waits=True):
                act.wait_ge(raw_landed[slot], base * (DMA // RAW) + DMA)
                if waits:
                    act.wait_ge(tiles_multiplied, base * TILES + (slot + 1 - PARTS) * TILES)
                nc.scalar.activation(hi[:, slot % PARTS], raw[:, slot], ACT.Copy).then_inc(hi_ready, 1)

            def drain(g, half):
                for t in range(TILES):
                    act.wait_ge(tiles_multiplied, x_complete(g, t))
                    nc.scalar.activation(s_hi[:, g * TILES + t], acc[:, half, t], ACT.Copy).then_inc(s_hi_ready, 1)

            def tile_std(g, t):
                act.wait_ge(var_ready, g * TILES + (t + 1))
                nc.scalar.activation(std[:, t], mean_var[:, t, 1:2], ACT.Sqrt, bias=eps[:]).then_inc(std_ready, 1)

            for c in range(X_CHUNKS):
                act.wait_ge(w_landed[c], DMA)
                nc.scalar.activation(w_hi[:, c * KB:(c + 1) * KB], w_raw[:, c * KB:(c + 1) * KB],
                                     ACT.Copy).then_inc(w_hi_ready, 1)
                split(0, c, waits=False)
            for slot in range(X_CHUNKS, RAW):
                split(0, slot)
            drain(0, 0)
            with act.Fori(1, GROUPS // 2) as q:
                split(q * RAW, 0)
                split(q * RAW, 1)
                drain(q * 2 - 1, 1)
                split(q * RAW, 2)
                split(q * RAW, 3)
                drain(q * 2, 0)
            split(XN, 0)
            split(XN, 1)
            drain(GROUPS - 1, 1)
            split(XN, 2)
            split(XN, 3)
            with act.Fori(XN + RAW, XN + A_CHUNKS, RAW) as n:
                for slot in range(RAW):
                    split(n, slot)
            act.wait_ge(eps_ready, 1)
            with act.Fori(1, GROUPS) as g:
                first = g * A_CHUNKS + XN
                for slot in range(RAW):
                    split(first, slot)
                    if slot >= 1:
                        tile_std(g - 1, slot - 1)
                split(first + RAW, 0)
                tile_std(g - 1, TILES - 1)
                for slot in range(1, RAW):
                    split(first + RAW, slot)
                with act.Fori(2 * RAW, A_CHUNKS, RAW) as c:
                    for slot in range(RAW):
                        split(first + c, slot)
            for t in range(TILES):
                tile_std(GROUPS - 1, t)

        @block.vector
        def _(dve):
            def split(base, slot):
                dve.wait_ge(hi_ready, base + (slot + 1))
                nc.vector.tensor_tensor(lo[:, slot % PARTS], raw[:, slot], hi[:, slot % PARTS].bitcast(fp32),
                                        ALU.subtract).then_inc(lo_ready, 1)

            def drain(g, half):
                for t in range(TILES):
                    dve.wait_ge(s_hi_ready, g * TILES + (t + 1))
                    nc.vector.tensor_tensor(s_lo[:, g * TILES + t], acc[:, half, t],
                                            s_hi[:, g * TILES + t].bitcast(fp32),
                                            ALU.subtract).then_inc(banks_drained, 1)

            def norm(g, half, t):
                k = g * TILES + (t + 1)
                y = rows[:, half, t]
                if t == 0:
                    dve.wait_ge(residual_ready, g + 1)
                dve.wait_ge(tiles_multiplied, a_complete(g, t))
                nc.vector.tensor_tensor(y, acc[:, half, t], y, ALU.add).then_inc(banks_drained, 1)
                dve.wait_ge(banks_drained, k + GROUPS * TILES)
                nc.vector.bn_stats(stats[:, t], y)
                dve.drain()
                nc.vector.bn_aggr(mean_var[:, t], stats[:, t]).then_inc(var_ready, 1)
                dve.wait_ge(std_ready, k)
                nc.vector.reciprocal(rstd[:, t], std[:, t]).then_inc(rstd_ready, 1)
                dve.wait_ge(rstd_ready, k)
                nc.vector.tensor_scalar(y, y, mean_var[:, t, 0:1], rstd[:, t], ALU.subtract,
                                        ALU.mult).then_inc(normalized, 1)

            for c in range(X_CHUNKS):
                dve.wait_ge(w_hi_ready, c + 1)
                nc.vector.tensor_tensor(w_lo[:, c * KB:(c + 1) * KB], w_raw[:, c * KB:(c + 1) * KB],
                                        w_hi[:, c * KB:(c + 1) * KB].bitcast(fp32),
                                        ALU.subtract).then_inc(w_lo_ready, 1)
                split(0, c)
            for slot in range(X_CHUNKS, RAW):
                split(0, slot)
            drain(0, 0)
            with dve.Fori(1, GROUPS // 2) as q:
                split(q * RAW, 0)
                split(q * RAW, 1)
                drain(q * 2 - 1, 1)
                split(q * RAW, 2)
                split(q * RAW, 3)
                drain(q * 2, 0)
            split(XN, 0)
            split(XN, 1)
            drain(GROUPS - 1, 1)
            split(XN, 2)
            split(XN, 3)
            with dve.Fori(XN + RAW, XN + A_CHUNKS, RAW) as n:
                for slot in range(RAW):
                    split(n, slot)

            def group(g, done_half):
                first = g * A_CHUNKS + XN
                for slot in range(RAW):
                    split(first, slot)
                    if slot >= 1:
                        norm(g - 1, done_half, slot - 1)
                split(first + RAW, 0)
                norm(g - 1, done_half, TILES - 1)
                for slot in range(1, RAW):
                    split(first + RAW, slot)
                with dve.Fori(2 * RAW, A_CHUNKS, RAW) as c:
                    for slot in range(RAW):
                        split(first + c, slot)

            with dve.Fori(0, GROUPS // 2 - 1) as i:
                group(i * 2 + 1, 0)
                group(i * 2 + 2, 1)
            group(GROUPS - 1, 0)
            for t in range(TILES):
                norm(GROUPS - 1, 1, t)

        @block.tensor
        def _(pe):
            def chunk(n, slot, half, moving_hi, moving_lo, first, last):
                pe.wait_ge(lo_ready, n + 1)
                for t in range(TILES):
                    cut = slice(t * P, (t + 1) * P)
                    for b in range(KB):
                        start, stop = first and b == 0, last and b == KB - 1
                        nc.tensor.matmul(acc[:, half, t], hi[:, slot, b, cut], moving_hi(b), start=start, stop=False)
                        nc.tensor.matmul(acc[:, half, t], hi[:, slot, b, cut], moving_lo(b), start=False, stop=False)
                        mm = nc.tensor.matmul(acc[:, half, t], lo[:, slot, b, cut], moving_hi(b), start=False,
                                              stop=stop)
                    mm.then_inc(tiles_multiplied, 1)

            def x_group(g, half):
                for c in range(X_CHUNKS):
                    if isinstance(g, int) and g == 0:
                        pe.wait_ge(w_lo_ready, c + 1)
                    chunk(g * X_CHUNKS + c, c % PARTS, half, lambda b: w_hi[:, c * KB + b], lambda b: w_lo[:, c * KB + b],
                          c == 0, c == X_CHUNKS - 1)

            x_group(0, 0)
            x_group(1, 1)
            with pe.Fori(1, GROUPS // 2) as i:
                for half in range(2):
                    pe.wait_ge(banks_drained, i * (2 * TILES) + (half - 1) * TILES)
                    x_group(i * 2 + half, half)

            def a_group(g, half):
                n = g * A_CHUNKS + XN

                def a_chunk(c, slot, first, last):
                    pe.wait_ge(banks_drained, c * KB + KB)
                    chunk(n + c, slot, half, lambda b: s_hi[:, c * KB + b], lambda b: s_lo[:, c * KB + b], first, last)

                pe.wait_ge(banks_drained, (g + (GROUPS - 1)) * TILES)
                for slot in range(PARTS):
                    a_chunk(slot, slot, slot == 0, False)
                with pe.Fori(1, A_CHUNKS // PARTS - 1) as k:
                    for slot in range(PARTS):
                        a_chunk(k * PARTS + slot, slot, False, False)
                for slot in range(PARTS):
                    a_chunk(A_CHUNKS - PARTS + slot, slot, False, slot == PARTS - 1)

            with pe.Fori(0, GROUPS // 2) as i:
                for half in range(2):
                    a_group(i * 2 + half, half)


_OUTS = [((4096, 512), 'float32')]


def _chunks(a, kb=2, permute=False):
    import numpy as _np
    n, k = a.shape
    rows = 512
    if permute:
        v = a.reshape(n // rows, 128, rows // 128, k // (128 * kb), kb, 128).transpose(0, 3, 5, 4, 2, 1)
    else:
        v = a.reshape(n // rows, rows // 128, 128, k // (128 * kb), kb, 128).transpose(0, 3, 5, 4, 1, 2)
    return _np.ascontiguousarray(v).reshape(-1, 128, kb, rows)


def kernel(x, adj, L0_gnn_weight, L0_gnn_bias):
    import numpy as _np
    import concourse.bacc as _bacc
    from concourse import mybir as _mybir
    from concourse.bass_utils import run_bass_kernel_spmd as _run

    nc = _bacc.Bacc("TRN2", target_bir_lowering=False, num_devices=1)
    x, adj = _np.asarray(x), _np.asarray(adj)
    ins = {
        "x": _np.ascontiguousarray(x),
        "xT": _chunks(x),
        "adjT": _chunks(adj, permute=True),
        "weight": _np.ascontiguousarray(L0_gnn_weight),
        "bias": _np.ascontiguousarray(L0_gnn_bias),
    }
    arrays, args = {}, []
    for name, a in ins.items():
        arrays[f"in_{name}_dram"] = a
        args.append(nc.dram_tensor(f"in_{name}_dram", a.shape, _mybir.dt.from_np(a.dtype), kind="ExternalInput").ap())
    for i, (shape, dtype) in enumerate(_OUTS):
        dt = _mybir.dt.from_np(_np.dtype(dtype))
        args.append(nc.dram_tensor(f"out_{i}_dram", shape, dt, kind="ExternalOutput").ap())
    gnn_residual_layernorm(nc, *args)
    r = _run(nc, [arrays], core_ids=[0])
    return r.results[0]["out_0_dram"]
```

```python
import concourse.bass as bass
from concourse import mybir
from contextlib import ExitStack

P = 128


def gnn_residual_layernorm(nc: bass.Bass, x: bass.AP, xT: bass.AP, adjT: bass.AP, weight: bass.AP,
                           bias: bass.AP, out: bass.AP):
    fp32 = mybir.dt.float32
    fp32r = mybir.dt.float32r
    ALU = mybir.AluOpType
    ACT = mybir.ActivationFunctionType

    N, F = x.shape
    ROWS = adjT.shape[3]
    TILES = ROWS // P
    KB = adjT.shape[2]
    GROUPS = N // ROWS
    X_CHUNKS = F // P // KB
    A_CHUNKS = N // P // KB
    RAW = 4
    PARTS = 2
    XN = GROUPS * X_CHUNKS
    LAST = XN + GROUPS * A_CHUNKS - RAW
    EPS = 1e-5
    RSTD_STEPS = 3
    WARM_UP = 8
    TOGETHER = PARTS + 1
    DMA = 16
    assert X_CHUNKS == PARTS and A_CHUNKS % RAW == 0 and XN % RAW == 0 and F <= 512

    ctx = ExitStack()
    with ctx:
        def sb(name, shape, dt=fp32):
            return ctx.enter_context(nc.sbuf_tensor(name, shape, dt))

        def sem(name):
            return ctx.enter_context(nc.semaphore(name))

        raw = sb("raw", [P, RAW, KB, ROWS])
        hi = sb("hi", [P, PARTS, KB, ROWS], fp32r)
        lo = sb("lo", [P, PARTS, KB, ROWS], fp32r)
        w_hi = sb("w_hi", [P, F // P, F], fp32r)
        w_lo = sb("w_lo", [P, F // P, F], fp32r)
        s_hi = sb("s_hi", [P, N // P, F], fp32r)
        s_lo = sb("s_lo", [P, N // P, F], fp32r)
        bias_all = sb("bias_all", [P, F])
        rows = sb("rows", [P, 2, TILES, F])
        w_raw = rows[:, 0]
        stats = sb("stats", [P, TILES, 6])
        mean_var = sb("mean_var", [P, TILES, 2])
        quarter = sb("quarter", [P, TILES, 1])
        root = sb("root", [P, TILES, 1])
        inverse = sb("inverse", [P, TILES, 1])
        std = sb("std", [P, TILES, 1])
        rstd = sb("rstd", [P, TILES, 1])
        zeros = sb("zeros", [P, F], mybir.dt.bfloat16)
        acc = ctx.enter_context(nc.psum_tensor("acc", [P, 2, TILES, F], fp32))

        w_landed = [sem(f"w_landed{b}") for b in range(F // P)]
        block_landed = [sem(f"block_landed{c}") for c in range(X_CHUNKS)]
        raw_landed = [sem(f"raw_landed{r}") for r in range(RAW)]
        bias_landed = sem("bias_landed")
        zeros_ready = sem("zeros_ready")
        x_landed = sem("x_landed")
        w_hi_ready = sem("w_hi_ready")
        w_lo_ready = sem("w_lo_ready")
        block_hi_ready = sem("block_hi_ready")
        block_lo_ready = sem("block_lo_ready")
        hi_ready = sem("hi_ready")
        lo_ready = sem("lo_ready")
        tiles_multiplied = sem("tiles_multiplied")
        s_hi_ready = sem("s_hi_ready")
        banks_drained = sem("banks_drained")
        residual_ready = sem("residual_ready")
        mean_var_ready = sem("mean_var_ready")
        quarter_ready = sem("quarter_ready")
        root_ready = sem("root_ready")
        rstd_steps = sem("rstd_steps")
        normalized = sem("normalized")
        stored = sem("stored")
        last_stored = sem("last_stored")

        x_rows = x.rearrange("(g p t) f -> g p t f", p=P, t=TILES)
        out_rows = out.rearrange("(g p t) f -> g p t f", p=P, t=TILES)
        w_rows = weight.rearrange("(b p) f -> p b f", p=P)

        def x_complete(g, t):
            return g * (X_CHUNKS * TILES) + ((X_CHUNKS - 1) * TILES + t + 1)

        def a_complete(g, t):
            if isinstance(g, int) and g == GROUPS - 1:
                return (g * A_CHUNKS + XN + A_CHUNKS - TOGETHER) * TILES + TOGETHER * (t + 1)
            return g * (A_CHUNKS * TILES) + ((XN + A_CHUNKS - 1) * TILES + t + 1)

        def late(parts, slot):
            at = slot % PARTS
            return parts[:, at * KB:(at + 1) * KB]

        block = ctx.enter_context(nc.Block())

        @block.sync
        def _(sp):
            for c in range(X_CHUNKS):
                for b in range(KB):
                    w_block = c * KB + b
                    landed = raw_landed[c] if b == KB - 1 else block_landed[c]
                    sp.dma_start(w_raw[:, w_block], w_rows[:, w_block]).then_inc(w_landed[w_block], DMA)
                    sp.dma_start(raw[:, c, b], xT[c, :, b]).then_inc(landed, DMA)
            for r in range(X_CHUNKS, RAW):
                sp.dma_start(raw[:, r], xT[r]).then_inc(raw_landed[r], DMA)
            with sp.Fori(1, XN // RAW) as q:
                for r in range(RAW):
                    sp.wait_ge(lo_ready, q * RAW + (r + 1 - RAW))
                    sp.dma_start(raw[:, r], xT[q * RAW + r]).then_inc(raw_landed[r], DMA)
            with sp.Fori(0, GROUPS * A_CHUNKS // RAW) as q:
                for r in range(RAW):
                    sp.wait_ge(lo_ready, q * RAW + (XN + r + 1 - RAW))
                    sp.dma_start(raw[:, r], adjT[q * RAW + r]).then_inc(raw_landed[r], DMA)
            g = GROUPS - 1
            for t in range(TILES):
                sp.wait_ge(normalized, g * TILES + t + 1)
                sp.dma_start(out_rows[g, :, t], rows[:, g % 2, t]).then_inc(last_stored, DMA)
            sp.wait_ge(last_stored, TILES * DMA)

        @block.gpsimd
        def _(pool):
            pool.dma_start(bias_all[:], bias.unsqueeze(0).to_broadcast([P, F])).then_inc(bias_landed, DMA)
            pool.wait_ge(bias_landed, DMA)
            pool.wait_ge(w_lo_ready, F // P)

            def prepare(g, slot):
                pool.dma_start(rows[:, slot], x_rows[g]).then_inc(x_landed, DMA)
                pool.wait_ge(x_landed, (g + 1) * DMA)
                for t in range(TILES):
                    last = nc.gpsimd.tensor_tensor(rows[:, slot, t], rows[:, slot, t], bias_all[:], ALU.add)
                last.then_inc(residual_ready, 1)

            def store(g, slot):
                pool.wait_ge(normalized, (g + 1) * TILES)
                pool.dma_start(out_rows[g], rows[:, slot]).then_inc(stored, DMA)
                pool.wait_ge(stored, (g + 1) * DMA)

            prepare(0, 0)
            prepare(1, 1)
            with pool.Fori(0, GROUPS // 2 - 1) as i:
                for h in range(2):
                    store(i * 2 + h, h)
                    prepare(i * 2 + (2 + h), h)
            store(GROUPS - 2, 0)

        @block.scalar
        def _(act):
            def split(base, slot):
                act.wait_ge(raw_landed[slot], base * (DMA // RAW) + DMA)
                act.wait_ge(tiles_multiplied, base * TILES + (slot + 1 - PARTS) * TILES)
                nc.scalar.activation(hi[:, slot % PARTS], raw[:, slot], ACT.Copy).then_inc(hi_ready, 1)

            def drain(g, half):
                for t in range(TILES):
                    act.wait_ge(tiles_multiplied, x_complete(g, t))
                    nc.scalar.activation(s_hi[:, g * TILES + t], acc[:, half, t], ACT.Copy).then_inc(s_hi_ready, 1)

            def tile_root(g, t):
                act.wait_ge(quarter_ready, g * TILES + (t + 1))
                nc.scalar.activation(root[:, t], quarter[:, t], ACT.Sqrt).then_inc(root_ready, 1)

            for c in range(X_CHUNKS):
                for b in range(KB):
                    landed, ready = (raw_landed, hi_ready) if b == KB - 1 else (block_landed, block_hi_ready)
                    act.wait_ge(landed[c], DMA)
                    nc.scalar.activation(hi[:, c, b], raw[:, c, b], ACT.Copy).then_inc(ready, 1)
            for slot in range(X_CHUNKS, RAW):
                split(0, slot)
            drain(0, 0)
            with act.Fori(1, GROUPS // 2) as q:
                split(q * RAW, 0)
                split(q * RAW, 1)
                drain(q * 2 - 1, 1)
                split(q * RAW, 2)
                split(q * RAW, 3)
                drain(q * 2, 0)
            split(XN, 0)
            split(XN, 1)
            drain(GROUPS - 1, 1)
            split(XN, 2)
            split(XN, 3)
            with act.Fori(XN + RAW, XN + A_CHUNKS, RAW) as n:
                for slot in range(RAW):
                    split(n, slot)

            def group(g, last_group=False):
                first = g * A_CHUNKS + XN
                for slot in range(RAW):
                    split(first, slot)
                    if slot >= 1:
                        tile_root(g - 1, slot - 1)
                split(first + RAW, 0)
                tile_root(g - 1, TILES - 1)
                for slot in range(1, RAW):
                    split(first + RAW, slot)
                with act.Fori(2, A_CHUNKS // RAW - last_group) as q:
                    for slot in range(RAW):
                        split(first + q * RAW, slot)

            with act.Fori(1, GROUPS - 1) as g:
                group(g)
            group(GROUPS - 1, last_group=True)
            for slot in range(PARTS):
                split(LAST, slot)
            for slot in range(PARTS, RAW):
                act.wait_ge(raw_landed[slot], LAST * (DMA // RAW) + DMA)
                nc.scalar.activation(late(w_hi, slot), raw[:, slot], ACT.Copy).then_inc(hi_ready, 1)
            for t in range(TILES):
                tile_root(GROUPS - 1, t)

        @block.vector
        def _(dve):
            def split(base, slot):
                dve.wait_ge(hi_ready, base + (slot + 1))
                nc.vector.tensor_tensor(lo[:, slot % PARTS], raw[:, slot], hi[:, slot % PARTS].bitcast(fp32),
                                        ALU.subtract).then_inc(lo_ready, 1)

            def drain(g, half):
                for t in range(TILES):
                    dve.wait_ge(s_hi_ready, g * TILES + (t + 1))
                    nc.vector.tensor_tensor(s_lo[:, g * TILES + t], acc[:, half, t],
                                            s_hi[:, g * TILES + t].bitcast(fp32),
                                            ALU.subtract).then_inc(banks_drained, 1)

            def norm(g, half, t):
                k = g * TILES + (t + 1)
                y = rows[:, half, t]
                if t == 0:
                    dve.wait_ge(residual_ready, g + 1)
                dve.wait_ge(tiles_multiplied, a_complete(g, t))
                nc.vector.tensor_tensor(y, acc[:, half, t], y, ALU.add).then_inc(banks_drained, 1)
                dve.wait_ge(banks_drained, k + GROUPS * TILES)
                nc.vector.bn_stats(stats[:, t], y)
                dve.drain()
                nc.vector.bn_aggr(mean_var[:, t], stats[:, t]).then_inc(mean_var_ready, 1)
                dve.wait_ge(mean_var_ready, k)
                nc.vector.tensor_scalar(quarter[:, t], mean_var[:, t, 1:2], EPS, 0.25, ALU.add,
                                        ALU.mult).then_inc(quarter_ready, 1)
                done = g * (TILES * RSTD_STEPS) + t * RSTD_STEPS
                dve.wait_ge(root_ready, k)
                nc.vector.reciprocal(inverse[:, t], root[:, t]).then_inc(rstd_steps, 1)
                dve.wait_ge(rstd_steps, done + 1)
                nc.vector.tensor_scalar(std[:, t], quarter[:, t], inverse[:, t], root[:, t], ALU.mult,
                                        ALU.add).then_inc(rstd_steps, 1)
                dve.wait_ge(rstd_steps, done + 2)
                nc.vector.reciprocal(rstd[:, t], std[:, t]).then_inc(rstd_steps, 1)
                dve.wait_ge(rstd_steps, done + 3)
                nc.vector.tensor_scalar(y, y, mean_var[:, t, 0:1], rstd[:, t], ALU.subtract,
                                        ALU.mult).then_inc(normalized, 1)

            nc.vector.memset(zeros[:], 0.0).then_inc(zeros_ready, 1)
            for c in range(X_CHUNKS):
                for b in range(KB):
                    w_block = c * KB + b
                    hi_done, lo_done = (hi_ready, lo_ready) if b == KB - 1 else (block_hi_ready, block_lo_ready)
                    dve.wait_ge(w_landed[w_block], DMA)
                    nc.vector.tensor_copy(w_hi[:, w_block], w_raw[:, w_block]).then_inc(w_hi_ready, 1)
                    dve.wait_ge(w_hi_ready, w_block + 1)
                    nc.vector.tensor_tensor(w_lo[:, w_block], w_raw[:, w_block], w_hi[:, w_block].bitcast(fp32),
                                            ALU.subtract).then_inc(w_lo_ready, 1)
                    dve.wait_ge(hi_done, c + 1)
                    nc.vector.tensor_tensor(lo[:, c, b], raw[:, c, b], hi[:, c, b].bitcast(fp32),
                                            ALU.subtract).then_inc(lo_done, 1)
            for slot in range(X_CHUNKS, RAW):
                split(0, slot)
            drain(0, 0)
            with dve.Fori(1, GROUPS // 2) as q:
                split(q * RAW, 0)
                split(q * RAW, 1)
                drain(q * 2 - 1, 1)
                split(q * RAW, 2)
                split(q * RAW, 3)
                drain(q * 2, 0)
            split(XN, 0)
            split(XN, 1)
            drain(GROUPS - 1, 1)
            split(XN, 2)
            split(XN, 3)
            with dve.Fori(XN + RAW, XN + A_CHUNKS, RAW) as n:
                for slot in range(RAW):
                    split(n, slot)

            def group(g, done_half, last_group=False):
                first = g * A_CHUNKS + XN
                for slot in range(RAW):
                    split(first, slot)
                    if slot >= 1:
                        norm(g - 1, done_half, slot - 1)
                split(first + RAW, 0)
                norm(g - 1, done_half, TILES - 1)
                for slot in range(1, RAW):
                    split(first + RAW, slot)
                with dve.Fori(2, A_CHUNKS // RAW - last_group) as q:
                    for slot in range(RAW):
                        split(first + q * RAW, slot)

            with dve.Fori(0, GROUPS // 2 - 1) as i:
                group(i * 2 + 1, 0)
                group(i * 2 + 2, 1)
            group(GROUPS - 1, 0, last_group=True)
            for slot in range(PARTS):
                split(LAST, slot)
            for slot in range(PARTS, RAW):
                dve.wait_ge(hi_ready, LAST + slot + 1)
                nc.vector.tensor_tensor(late(w_lo, slot), raw[:, slot], late(w_hi, slot).bitcast(fp32),
                                        ALU.subtract).then_inc(lo_ready, 1)
            for t in range(TILES):
                norm(GROUPS - 1, 1, t)

        @block.tensor
        def _(pe):
            def products(t, out_tile, block_hi, block_lo, moving_hi, moving_lo, start, stop):
                cut = slice(t * P, (t + 1) * P)
                nc.tensor.matmul(out_tile, block_hi[:, cut], moving_hi, start=start, stop=False)
                nc.tensor.matmul(out_tile, block_hi[:, cut], moving_lo, start=False, stop=False)
                return nc.tensor.matmul(out_tile, block_lo[:, cut], moving_hi, start=False, stop=stop)

            def x_chunk(n, c, half):
                pe.wait_ge(lo_ready, n + 1)
                for t in range(TILES):
                    for b in range(KB):
                        k = c * KB + b
                        last = products(t, acc[:, half, t], hi[:, c, b], lo[:, c, b], w_hi[:, k], w_lo[:, k],
                                        k == 0, k == F // P - 1)
                    last.then_inc(tiles_multiplied, 1)

            pe.wait_ge(zeros_ready, 1)
            for _ in range(WARM_UP):
                nc.tensor.matmul(acc[:, 1, 0], zeros[:, 0:P], zeros[:], start=True, stop=True)
            cuts = [slice(t * P, (t + 1) * P) for t in range(TILES)]
            for c in range(X_CHUNKS):
                for b in range(KB):
                    k = c * KB + b
                    hi_done, lo_done = (hi_ready, lo_ready) if b == KB - 1 else (block_hi_ready, block_lo_ready)
                    pe.wait_ge(w_hi_ready, k + 1)
                    pe.wait_ge(hi_done, c + 1)
                    for t in range(TILES):
                        nc.tensor.matmul(acc[:, 0, t], hi[:, c, b, cuts[t]], w_hi[:, k], start=k == 0, stop=False)
                    pe.wait_ge(w_lo_ready, k + 1)
                    for t in range(TILES):
                        nc.tensor.matmul(acc[:, 0, t], hi[:, c, b, cuts[t]], w_lo[:, k], start=False, stop=False)
                    pe.wait_ge(lo_done, c + 1)
                    for t in range(TILES):
                        mm = nc.tensor.matmul(acc[:, 0, t], lo[:, c, b, cuts[t]], w_hi[:, k], start=False,
                                              stop=k == F // P - 1)
                        if b == KB - 1:
                            mm.then_inc(tiles_multiplied, 1)
            for c in range(X_CHUNKS):
                x_chunk(X_CHUNKS + c, c, 1)
            with pe.Fori(1, GROUPS // 2) as i:
                for half in range(2):
                    pe.wait_ge(banks_drained, i * (2 * TILES) + (half - 1) * TILES)
                    for c in range(X_CHUNKS):
                        x_chunk(i * (2 * X_CHUNKS) + (half * X_CHUNKS + c), c, half)

            def a_chunk(n, c, slot, half, first=False, last=False):
                pe.wait_ge(lo_ready, n + 1)
                pe.wait_ge(banks_drained, c * KB + KB)
                for t in range(TILES):
                    for b in range(KB):
                        k = c * KB + b
                        mm = products(t, acc[:, half, t], hi[:, slot, b], lo[:, slot, b], s_hi[:, k], s_lo[:, k],
                                      first and b == 0, last and b == KB - 1)
                    mm.then_inc(tiles_multiplied, 1)

            def a_group(g, half, last_group=False):
                n = g * A_CHUNKS + XN
                pe.wait_ge(banks_drained, (g + (GROUPS - 1)) * TILES)
                for slot in range(PARTS):
                    a_chunk(n + slot, slot, slot, half, first=slot == 0)
                with pe.Fori(1, A_CHUNKS // PARTS - 1 - last_group) as i:
                    for slot in range(PARTS):
                        a_chunk(n + i * PARTS + slot, i * PARTS + slot, slot, half)
                c = A_CHUNKS - PARTS
                if not last_group:
                    for slot in range(PARTS):
                        a_chunk(n + (c + slot), c + slot, slot, half, last=slot == PARTS - 1)
                    return
                a_chunk(n + c - PARTS, c - PARTS, 0, half)
                ends = [(c - 1, hi[:, 1], lo[:, 1])]
                ends += [(c + at, late(w_hi, at), late(w_lo, at)) for at in range(PARTS)]
                for t in range(TILES):
                    for j, chunk_hi, chunk_lo in ends:
                        if t == 0:
                            pe.wait_ge(lo_ready, n + j + 1)
                        for b in range(KB):
                            k = j * KB + b
                            mm = products(t, acc[:, half, t], chunk_hi[:, b], chunk_lo[:, b], s_hi[:, k], s_lo[:, k],
                                          False, k == N // P - 1)
                        mm.then_inc(tiles_multiplied, 1)

            with pe.Fori(0, GROUPS // 2 - 1) as i:
                for half in range(2):
                    a_group(i * 2 + half, half)
            a_group(GROUPS - 2, 0)
            a_group(GROUPS - 1, 1, last_group=True)


_OUTS = [((4096, 512), 'float32')]


def _chunks(a, kb=2, permute=False):
    import numpy as _np
    n, k = a.shape
    rows = 512
    if permute:
        v = a.reshape(n // rows, 128, rows // 128, k // (128 * kb), kb, 128).transpose(0, 3, 5, 4, 2, 1)
    else:
        v = a.reshape(n // rows, rows // 128, 128, k // (128 * kb), kb, 128).transpose(0, 3, 5, 4, 1, 2)
    return _np.ascontiguousarray(v).reshape(-1, 128, kb, rows)


def kernel(x, adj, L0_gnn_weight, L0_gnn_bias):
    import numpy as _np
    import concourse.bacc as _bacc
    from concourse import mybir as _mybir
    from concourse.bass_utils import run_bass_kernel_spmd as _run

    nc = _bacc.Bacc("TRN2", target_bir_lowering=False, num_devices=1)
    x, adj = _np.asarray(x), _np.asarray(adj)
    ins = {
        "x": _np.ascontiguousarray(x),
        "xT": _chunks(x),
        "adjT": _chunks(adj, permute=True),
        "weight": _np.ascontiguousarray(L0_gnn_weight),
        "bias": _np.ascontiguousarray(L0_gnn_bias),
    }
    arrays, args = {}, []
    for name, a in ins.items():
        arrays[f"in_{name}_dram"] = a
        args.append(nc.dram_tensor(f"in_{name}_dram", a.shape, _mybir.dt.from_np(a.dtype), kind="ExternalInput").ap())
    for i, (shape, dtype) in enumerate(_OUTS):
        dt = _mybir.dt.from_np(_np.dtype(dtype))
        args.append(nc.dram_tensor(f"out_{i}_dram", shape, dt, kind="ExternalOutput").ap())
    gnn_residual_layernorm(nc, *args)
    r = _run(nc, [arrays], core_ids=[0])
    return r.results[0]["out_0_dram"]
```
